# Optimizing a Trainium2 kernel written in Bass

```python
import numpy as np
import jax
import jax.numpy as jnp

def _softmax(x, axis=-1):
    return jax.nn.softmax(x, axis=axis)

def _gelu(x):
    return jax.nn.gelu(x, approximate=True)

def _silu(x):
    return jax.nn.silu(x)

def _sigmoid(x):
    return jax.nn.sigmoid(x)

def _layernorm(x, axis=-1, eps=1e-05):
    m = jnp.mean(x, axis=axis, keepdims=True)
    v = jnp.var(x, axis=axis, keepdims=True)
    return (x - m) / jnp.sqrt(v + eps)

def _scatter_add(tgt, idx, src, axis=0):
    return tgt.at[idx].add(src)

def _segment_sum(src, seg, n):
    return jax.ops.segment_sum(src, seg, n)
kernel_name = 'mk_conv_preact_d1_conv_nchw256_r4_8531d2'

def setup_inputs(seed: int=0):
    np.random.seed(seed)
    _w = jnp.asarray

    def _rec_inputs():
        import jax
        import jax.numpy as jnp
        _gk = jax.random.key(seed)
        x = -0.0003929 + 0.9999 * jax.random.normal(jax.random.fold_in(_gk, 1), (16, 64, 16, 16), jnp.float32)
        return x
    x = _rec_inputs()

    def _L0_conv_setup():
        import jax, jax.numpy as jnp
        import numpy as np
        HEADS = 8
        DIM_HEAD = 16
        key = jax.random.key(seed)
        k1, k2, k3, k4 = jax.random.split(key, 4)
        dim, hidden = (64, HEADS * DIM_HEAD)
        x = jax.random.normal(k1, (16, dim, 16, 16), dtype=jnp.float32)
        w_qkv = jax.random.normal(k2, (hidden * 3, dim), dtype=jnp.float32) * (1.0 / np.sqrt(dim))
        w_out = jax.random.normal(k3, (dim, hidden), dtype=jnp.float32) * (1.0 / np.sqrt(hidden))
        b_out = jax.random.normal(k4, (dim,), dtype=jnp.float32) * 0.01
        return {'x': x, 'w_qkv': w_qkv, 'w_out': w_out, 'b_out': b_out}
    _L0_conv_all = _L0_conv_setup()
    _L0_conv_in = {k: v for k, v in _L0_conv_all.items() if k in ('w_qkv', 'w_out', 'b_out')}
    del _L0_conv_all
    return {'x': x, 'L0_conv_w_qkv': _L0_conv_in['w_qkv'], 'L0_conv_w_out': _L0_conv_in['w_out'], 'L0_conv_b_out': _L0_conv_in['b_out']}

def reference(x, L0_conv_w_qkv, L0_conv_w_out, L0_conv_b_out):
    import jax
    import jax.numpy as jnp

    def _L0_conv_ref(x, w_qkv, w_out, b_out):
        import jax, jax.numpy as jnp
        import numpy as np
        HEADS = 8
        DIM_HEAD = 16
        b, c, h, w = x.shape
        n = h * w
        xf = x.reshape(b, c, n)
        qkv = jnp.einsum('oc,bcn->bon', w_qkv, xf)
        qkv = qkv.reshape(b, 3, HEADS, DIM_HEAD, n)
        q, k, v = (qkv[:, 0], qkv[:, 1], qkv[:, 2])
        k = jax.nn.softmax(k, axis=-1)
        context = jnp.einsum('bhdn,bhen->bhde', k, v)
        out = jnp.einsum('bhde,bhdn->bhen', context, q)
        out = out.reshape(b, HEADS * DIM_HEAD, n)
        y = jnp.einsum('oc,bcn->bon', w_out, out) + b_out[None, :, None]
        return y.reshape(b, w_out.shape[0], h, w)

    def _gn(v, G=32, eps=1e-05):
        B_, C_, H_, W_ = v.shape
        g = v.reshape(B_, G, C_ // G, H_, W_)
        m = jnp.mean(g, axis=(2, 3, 4), keepdims=True)
        s = jnp.var(g, axis=(2, 3, 4), keepdims=True)
        return ((g - m) / jnp.sqrt(s + eps)).reshape(v.shape)

    def _ln_c(v, eps=1e-06):
        m = jnp.mean(v, axis=1, keepdims=True)
        s = jnp.var(v, axis=1, keepdims=True)
        return (v - m) / jnp.sqrt(s + eps)

    def _ln_t(v, eps=1e-05):
        m = jnp.mean(v, axis=-1, keepdims=True)
        s = jnp.var(v, axis=-1, keepdims=True)
        return (v - m) / jnp.sqrt(s + eps)

    def _to_tokens(v):
        B_, C_, H_, W_ = v.shape
        return v.reshape(B_, C_, H_ * W_).transpose(0, 2, 1)

    def _from_tokens(t, like):
        B_, C_, H_, W_ = like.shape
        return t.transpose(0, 2, 1).reshape(B_, C_, H_, W_)
    x = x + _L0_conv_ref(_gn(x), L0_conv_w_qkv, L0_conv_w_out, L0_conv_b_out)
    return x

_drawn_inputs = setup_inputs


def setup_inputs(seed=0):
    import zlib

    import numpy as np

    out = dict(_drawn_inputs(seed))
    spreads = {}
    factors = {'L0_conv_b_out': 5.426}
    for name, (base, spread) in spreads.items():
        noise = np.random.default_rng([zlib.crc32(name.encode()), seed]).standard_normal(out[name].shape)
        drawn = base * np.exp(spread * noise) if base else spread * noise
        out[name] = jnp.asarray(drawn.astype(out[name].dtype))
    for name, factor in factors.items():
        out[name] = (out[name] * factor).astype(out[name].dtype)
    return out
```

```python
import concourse.bass as bass
from concourse import mybir
from contextlib import ExitStack


def attention_kernel(nc, x, w_qkv, w_out, b_out, y):
    F32, BF16 = mybir.dt.float32, mybir.dt.bfloat16
    ALU = mybir.AluOpType
    EXP = mybir.ActivationFunctionType.Exp
    X = mybir.AxisListType.X

    BATCH, C, N = x.shape
    HID = w_out.shape[1]
    HEADS, DH = 8, HID // 8
    PAIRS = BATCH // 2
    CH = N // 128
    EPS = 1e-5
    PER_GROUP = 2

    STATS = [[0], [1], [2, 3], [4, 5], [6, 7]]
    GROUPS = [[0, 1, 2], [3, 4, 5], [6, 7]]
    LOADS = [[0], [1], [2, 3], [4, 5], [6, 7]]
    WARM = 9
    group_of = {p: g for g, ps in enumerate(GROUPS) for p in ps}
    load_of = {p: i for i, ps in enumerate(LOADS) for p in ps}

    with ExitStack() as ctx:
        def sb(name, shape, dt=F32):
            return ctx.enter_context(nc.sbuf_tensor(name, shape, dt))

        def bank(name):
            return ctx.enter_context(nc.psum_tensor(name + "_bank", [128, 512], F32))

        def sem(name):
            return ctx.enter_context(nc.semaphore(name))

        ident = sb("ident", [128, 128])
        neg_half = sb("neg_half", [128, 64, 2])
        head_mask = sb("head_mask", [128, HEADS])
        eps_row = sb("eps_row", [128, 2, 2])
        neg_power = sb("neg_power", [128, 2])
        zeros = sb("zeros", [128, 512], BF16)
        scrap = sb("scrap", [128, 1])
        wk = sb("wk", [HID, 2, C])
        wq = sb("wq", [HID, C])
        wv = sb("wv", [HID, 2, C])
        wo = sb("wo", [C, HID])
        bias = sb("bias", [128, 1])
        wkT = sb("wkT", [128, 2, HID])
        woM = sb("woM", [HID, HEADS, C])
        G = sb("G", [128, HEADS, C])
        x_sb = sb("x_sb", [128, PAIRS, N])
        xn = sb("xn", [128, PAIRS, N])
        stats6 = sb("stats6", [128, PAIRS, 6])
        mv = sb("mv", [128, PAIRS, 2])
        gmv = sb("gmv", [128, PAIRS, 2])
        dev = sb("dev", [128, PAIRS])
        var = sb("var", [128, PAIRS])
        rstd = sb("rstd", [128, PAIRS])
        nmax = sb("nmax", [128, BATCH])
        psum_d = sb("psum_d", [128, BATCH])
        rsum = sb("rsum", [128, BATCH])
        P = sb("P", [128, BATCH, N])
        PT = sb("PT", [128, PAIRS, 2, CH, HID])
        xT = sb("xT", [128, PAIRS, CH, 128])
        AT = sb("AT", [128, PAIRS, HID])
        BT = sb("BT", [128, PAIRS, HID])
        B = sb("B", [HID, PAIRS, 2, C])
        MT = sb("MT", [128, PAIRS, 2, C])
        y_sb = sb("y_sb", [128, PAIRS, N])

        k_bank = [bank("k0"), bank("k1")]
        pt_bank = [bank("pt0"), bank("pt1")]
        xt_bank = bank("xt")
        at_bank = bank("at")
        chain_bank = bank("chain")
        y_bank = bank("y")
        y_banks = {p: y_bank for p in range(PAIRS)}
        for i, p in enumerate(GROUPS[-1]):
            y_banks[p] = [k_bank[0], k_bank[1], y_bank][i % 3]

        x_in = [sem(f"x_in{i}") for i in range(len(LOADS))]
        wk_in, wq_in, wv_in, wo_in, bias_in = (sem(n) for n in ("wk_in", "wq_in", "wv_in", "wo_in", "bias_in"))
        zeros_set, ident_set, half_set, mask_set, misc_set, mt_zero, wk_zero = (
            sem(n) for n in ("zeros_set", "ident_set", "half_set", "mask_set", "misc_set", "mt_zero", "wk_zero"))
        wkT_ps, wkT_set, woT_ps, woM_set, g_ps, g_set = (
            sem(n) for n in ("wkT_ps", "wkT_set", "woT_ps", "woM_set", "g_ps", "g_set"))
        bn_done = sem("bn_done")
        mv_done = sem("mv_done")
        gmean_ps = sem("gmean_ps")
        gmv_done = sem("gmv_done")
        dev_done = sem("dev_done")
        var_done = sem("var_done")
        rstd_done = sem("rstd_done")
        xn_done = sem("xn_done")
        k_ps = sem("k_ps")
        max_done = sem("max_done")
        exp_done = sem("exp_done")
        xt_ps = sem("xt_ps")
        xt_done = sem("xt_done")
        pt_ps = sem("pt_ps")
        pt_done = sem("pt_done")
        at_ps = sem("at_ps")
        at_done = sem("at_done")
        bt_ps = sem("bt_ps")
        bt_done = sem("bt_done")
        rsum_done = sem("rsum_done")
        b_ps = sem("b_ps")
        b_done = sem("b_done")
        m_ps = sem("m_ps")
        m_done = [sem("m_done0"), sem("m_done1")]
        y_ps = sem("y_ps")
        y_done = sem("y_done")
        y_out = sem("y_out")

        x_v = x.rearrange("(p two) c n -> (two c) p n", two=2)
        y_v = y.rearrange("(p two) c n -> (two c) p n", two=2)

        block = ctx.enter_context(nc.Block())

        @block.sync
        def _(sp):
            for i, ps in enumerate(LOADS):
                sp.dma_start(x_sb[:, ps[0]:ps[-1] + 1, :], x_v[:, ps[0]:ps[-1] + 1, :]).then_inc(x_in[i], 16)
            for p in range(PAIRS):
                sp.wait_ge(y_done, p + 1)
                sp.dma_start(y_v[:, p, :], y_sb[:, p, :]).then_inc(y_out, 16)
            sp.wait_ge(y_out, 16 * PAIRS)

        @block.gpsimd
        def _(pool):
            def set_const(tile, value, *selects):
                nc.gpsimd.memset(tile, value).then_inc(misc_set, 1)
                steps[0] += 1
                for base, mult, pattern in selects:
                    pool.wait_ge(misc_set, steps[0])
                    last = nc.gpsimd.affine_select(out=tile, in_=tile, compare_op=ALU.is_ge, fill=0.0, base=base,
                                                   pattern=pattern, channel_multiplier=mult)
                    last.then_inc(misc_set, 1)
                    steps[0] += 1
                pool.wait_ge(misc_set, steps[0])

            steps = [0]
            nc.gpsimd.memset(zeros[:, :], 0.0).then_inc(zeros_set, 1)
            nc.gpsimd.memset(wkT[:, :, :], 0.0).then_inc(wk_zero, 1)
            set_const(ident[:, :], 1.0, (0, 1, [[-1, 128]]), (0, -1, [[1, 128]]))
            pool.nop().then_inc(ident_set, 1)
            set_const(neg_half[:, :, :], -1.0 / PER_GROUP, (0, 1, [[-2, 64], [0, 2]]), (1, -1, [[2, 64], [0, 2]]))
            set_const(neg_power[:, :], -0.5)
            set_const(eps_row[:, :, 0], 0.0)
            set_const(eps_row[:, :, 1], -EPS)
            pool.nop().then_inc(half_set, 1)
            set_const(head_mask[:, :], 1.0, (0, 1, [[-DH, HEADS]]), (DH - 1, -1, [[DH, HEADS]]))
            pool.nop().then_inc(mask_set, 1)

            def inverse_std(p):
                pool.wait_ge(var_done, p + 1)
                nc.gpsimd.tensor_tensor(rstd[:, p:p + 1], var[:, p:p + 1], neg_power[:, 0:1],
                                        ALU.pow).then_inc(rstd_done, 1)

            for p in range(PAIRS):
                inverse_std(p)
                if p == 1:
                    nc.gpsimd.memset(MT[:, :, :, :], 0.0).then_inc(mt_zero, 1)

        @block.scalar
        def _(act):
            act.dma_start(wk[:, 0, :], w_qkv[HID:2 * HID, :]).then_inc(wk_in, 16)
            act.dma_start(wk[:, 1, :], w_qkv[HID:2 * HID, :]).then_inc(wk_in, 16)
            act.dma_start(wo[:, :], w_out).then_inc(wo_in, 16)
            act.dma_start(wv[:, 0, :], w_qkv[2 * HID:3 * HID, :]).then_inc(wv_in, 16)
            act.dma_start(wv[:, 1, :], w_qkv[2 * HID:3 * HID, :]).then_inc(wv_in, 16)
            act.dma_start(wq[:, :], w_qkv[0:HID, :]).then_inc(wq_in, 16)
            act.dma_start(bias[0:C, :], b_out).then_inc(bias_in, 16)
            act.dma_start(bias[C:128, :], b_out).then_inc(bias_in, 16)
            act.wait_ge(zeros_set, 1)
            nc.scalar.activation(scrap[:, :], zeros[:, 0:1], EXP)
            act.wait_ge(wkT_ps, 1)
            act.wait_ge(wk_zero, 1)
            for half in range(2):
                rows = slice(C * half, C * half + C)
                nc.scalar.copy(wkT[rows, half, :], pt_bank[0][rows, 0:HID]).then_inc(wkT_set, 1)

            def exps(p):
                act.wait_ge(max_done, p + 1)
                for half in range(2):
                    b = 2 * p + half
                    nc.scalar.activation(P[:, b, :], k_bank[p % 2][:, half * N:(half + 1) * N], EXP,
                                         bias=nmax[:, b:b + 1], accum_out=psum_d[:, b:b + 1]).then_inc(exp_done, 1)

            def copy_pt(p):
                act.wait_ge(pt_ps, p + 1)
                nc.scalar.copy(PT[:, p, :, :, :], pt_bank[p % 2][:, :]).then_inc(pt_done, 1)

            def copy_xt(p):
                act.wait_ge(xt_ps, p + 1)
                nc.scalar.copy(xT[:, p, :, :], xt_bank[:, 0:CH * 128]).then_inc(xt_done, 1)

            def copy_at(g):
                ps = GROUPS[g]
                act.wait_ge(at_ps, ps[-1] + 1)
                nc.scalar.copy(AT[:, ps[0]:ps[-1] + 1, :], at_bank[:, 0:len(ps) * HID]).then_inc(at_done, 1)

            def copy_m(g, half):
                ps = GROUPS[g]
                rows = slice(C * half, C * half + C)
                act.wait_ge(m_ps, g + 1)
                act.wait_ge(mt_zero, 1)
                nc.scalar.copy(MT[rows, ps[0]:ps[-1] + 1, half, :],
                               chain_bank[rows, 0:len(ps) * C]).then_inc(m_done[half], 1)

            for s in range(PAIRS + 3):
                if s < PAIRS:
                    copy_xt(s)
                    exps(s)
                if 0 <= s - 1 < PAIRS:
                    copy_pt(s - 1)
                for g, ps in enumerate(GROUPS):
                    if ps[-1] == s - 2:
                        copy_at(g)
                        copy_m(g, 1)

        @block.vector
        def _(dve):
            def moments(p):
                dve.wait_ge(x_in[load_of[p]], 16)
                nc.vector.bn_stats(stats6[:, p, :], x_sb[:, p, :]).then_inc(bn_done, 1)
                dve.wait_ge(bn_done, p + 1)
                nc.vector.bn_aggr(mv[:, p, :], stats6[:, p, :]).then_inc(mv_done, 1)

            def variances(i):
                ps = STATS[i]
                lo, hi = ps[0], ps[-1] + 1
                dve.wait_ge(gmean_ps, i + 1)
                nc.vector.tensor_tensor(gmv[:, lo:hi, :], at_bank[:, 2 * lo:2 * hi], eps_row[:, 0:hi - lo, :],
                                        ALU.add).then_inc(gmv_done, 1)
                dve.wait_ge(gmv_done, i + 1)
                nc.vector.tensor_tensor(dev[:, lo:hi], mv[:, lo:hi, 0], gmv[:, lo:hi, 0],
                                        ALU.add).then_inc(dev_done, 1)
                dve.wait_ge(dev_done, i + 1)
                for p in ps:
                    nc.vector.scalar_tensor_tensor(var[:, p:p + 1], dev[:, p:p + 1], dev[:, p:p + 1], gmv[:, p, 1:2],
                                                   ALU.mult, ALU.subtract).then_inc(var_done, 1)

            def normalise(p):
                dve.wait_ge(rstd_done, p + 1)
                nc.vector.tensor_scalar(xn[:, p, :], x_sb[:, p, :], gmv[:, p, 0:1], rstd[:, p:p + 1],
                                        ALU.add, ALU.mult).then_inc(xn_done, 1)

            def maxima(p):
                dve.wait_ge(k_ps, p + 1)
                nc.vector.tensor_reduce(nmax[:, 2 * p:2 * p + 2], k_bank[p % 2][:, :].rearrange("d (h n) -> d h n", h=2),
                                        X, ALU.max, negate=True).then_inc(max_done, 1)

            def copy_bt(g):
                ps = GROUPS[g]
                dve.wait_ge(bt_ps, g + 1)
                nc.vector.tensor_copy(BT[:, ps[0]:ps[-1] + 1, :],
                                      chain_bank[:, 0:len(ps) * HID]).then_inc(bt_done, 1)

            def inverse_sums(g):
                lo, hi = 2 * GROUPS[g][0], 2 * GROUPS[g][-1] + 2
                dve.wait_ge(exp_done, hi)
                nc.vector.reciprocal(rsum[:, lo:hi], psum_d[:, lo:hi]).then_inc(rsum_done, 1)

            def scale_b(g):
                ps = GROUPS[g]
                n = 2 * len(ps)
                dve.wait_ge(b_ps, g + 1)
                dve.wait_ge(rsum_done, g + 1)
                nc.vector.tensor_tensor(B[:, ps[0]:ps[-1] + 1, :, :].rearrange("d p h o -> d (p h) o"),
                                        chain_bank[:, 0:n * C].rearrange("d (b o) -> d b o", b=n),
                                        rsum[:, 2 * ps[0]:2 * ps[0] + n].unsqueeze(2).to_broadcast([128, n, C]),
                                        ALU.mult).then_inc(b_done, 1)

            def copy_m(g, half):
                ps = GROUPS[g]
                rows = slice(C * half, C * half + C)
                dve.wait_ge(m_ps, g + 1)
                dve.wait_ge(mt_zero, 1)
                nc.vector.tensor_copy(MT[rows, ps[0]:ps[-1] + 1, half, :],
                                      chain_bank[rows, 0:len(ps) * C]).then_inc(m_done[half], 1)

            def residual(p):
                dve.wait_ge(y_ps, p + 1)
                if p == 0:
                    dve.wait_ge(bias_in, 32)
                nc.vector.scalar_tensor_tensor(y_sb[:, p, :], y_banks[p][:, 0:N], bias[:, :], x_sb[:, p, :],
                                               ALU.add, ALU.add).then_inc(y_done, 1)

            moments(0)
            moments(1)
            variances(0)
            moments(2)
            normalise(0)
            variances(1)
            moments(3)
            dve.wait_ge(woT_ps, 1)
            dve.wait_ge(mask_set, 1)
            nc.vector.tensor_tensor(woM[:, :, :], pt_bank[1][:, 0:C].unsqueeze(1).to_broadcast([128, HEADS, C]),
                                    head_mask[:, :].unsqueeze(2).to_broadcast([128, HEADS, C]),
                                    ALU.mult).then_inc(woM_set, 1)
            normalise(1)
            for s in range(PAIRS + 6):
                if s < PAIRS:
                    maxima(s)
                if s == 0:
                    variances(2)
                if s in (0, 1):
                    moments(4 + 2 * s)
                    moments(5 + 2 * s)
                    normalise(2 + s)
                    variances(3 + s)
                    if s == 0:
                        dve.wait_ge(g_ps, 1)
                        nc.vector.tensor_copy(G[:, :, :], chain_bank[:, :]).then_inc(g_set, 1)
                elif s + 2 < PAIRS:
                    normalise(s + 2)
                for g, ps in enumerate(GROUPS):
                    if ps[-1] == s - 2:
                        copy_bt(g)
                        inverse_sums(g)
                        scale_b(g)
                        copy_m(g, 0)
                        for p in ps:
                            residual(p)

        @block.tensor
        def _(pe):
            def transpose_x(p):
                pe.wait_ge(xn_done, p + 1)
                if p >= 1:
                    pe.wait_ge(xt_done, p)
                for ch in range(CH):
                    last = nc.tensor.transpose(xt_bank[:, ch * 128:(ch + 1) * 128],
                                               xn[:, p, ch * 128:(ch + 1) * 128], ident[:, :])
                last.then_inc(xt_ps, 1)

            def keys(p):
                pe.wait_ge(xn_done, p + 1)
                if p == 0:
                    pe.wait_ge(wkT_set, 2)
                if p >= 2:
                    pe.wait_ge(exp_done, 2 * (p - 1))
                for half in range(2):
                    last = nc.tensor.matmul(k_bank[p % 2][:, half * N:(half + 1) * N], wkT[:, half, :], xn[:, p, :],
                                            start=True, stop=True)
                last.then_inc(k_ps, 1)

            def transpose_p(p):
                pe.wait_ge(exp_done, 2 * p + 2)
                if p == 1:
                    pe.wait_ge(woM_set, 1)
                if p >= 2:
                    pe.wait_ge(pt_done, p - 1)
                for half in range(2):
                    for ch in range(CH):
                        c0 = (half * CH + ch) * 128
                        last = nc.tensor.transpose(pt_bank[p % 2][:, c0:c0 + 128],
                                                   P[:, 2 * p + half, ch * 128:(ch + 1) * 128], ident[:, :])
                last.then_inc(pt_ps, 1)

            def context(p):
                g = group_of[p]
                pe.wait_ge(pt_done, p + 1)
                pe.wait_ge(xt_done, p + 1)
                if p == 0:
                    pe.wait_ge(gmv_done, len(STATS))
                elif p == GROUPS[g][0]:
                    pe.wait_ge(at_done, g)
                c0 = (p - GROUPS[g][0]) * HID
                for ch in range(CH):
                    for half in range(2):
                        rows = slice(C * half, C * half + C)
                        last = nc.tensor.matmul(at_bank[rows, c0:c0 + HID], xT[:, p, ch, rows], PT[:, p, half, ch, :],
                                                start=(ch == 0), stop=(ch == CH - 1))
                last.then_inc(at_ps, 1)

            def heads(g):
                ps = GROUPS[g]
                pe.wait_ge(at_done, g + 1)
                if g == 0:
                    pe.wait_ge(g_set, 1)
                else:
                    for half in range(2):
                        pe.wait_ge(m_done[half], g)
                out = chain_bank[:, 0:len(ps) * HID].rearrange("o (p d) -> o p d", p=len(ps))
                for h in range(HEADS):
                    for half in range(2):
                        rows = slice(C * half, C * half + C)
                        last = nc.tensor.matmul(out[rows, :, h * DH:(h + 1) * DH], G[rows, h, :],
                                                AT[rows, ps[0]:ps[-1] + 1, h * DH:(h + 1) * DH],
                                                start=True, stop=True)
                last.then_inc(bt_ps, 1)

            def transpose_b(g):
                pe.wait_ge(bt_done, g + 1)
                for i, p in enumerate(GROUPS[g]):
                    last = nc.tensor.transpose(chain_bank[:, i * 128:(i + 1) * 128], BT[:, p, :], ident[:, :])
                last.then_inc(b_ps, 1)

            def project(g):
                ps = GROUPS[g]
                pe.wait_ge(b_done, g + 1)
                if g == 0:
                    pe.wait_ge(wq_in, 16)
                for half in range(2):
                    last = nc.tensor.matmul(chain_bank[C * half:C * half + C, 0:len(ps) * C], wq[:, :],
                                            B[:, ps[0]:ps[-1] + 1, half, :], start=True, stop=True)
                last.then_inc(m_ps, 1)

            def outputs(p):
                g = group_of[p]
                for half in range(2):
                    pe.wait_ge(m_done[half], g + 1)
                if y_banks[p] is y_bank:
                    before = [q for q in range(p) if y_banks[q] is y_bank]
                    if before:
                        pe.wait_ge(y_done, before[-1] + 1)
                else:
                    pe.wait_ge(exp_done, BATCH)
                nc.tensor.matmul(y_banks[p][:, 0:N], MT[:, p, :, :], xn[:, p, :],
                                 start=True, stop=True).then_inc(y_ps, 1)

            def group_means(i):
                ps = STATS[i]
                lo, hi = ps[0], ps[-1] + 1
                pe.wait_ge(mv_done, hi)
                if i == 0:
                    pe.wait_ge(half_set, 1)
                else:
                    pe.wait_ge(gmv_done, i)
                nc.tensor.matmul(at_bank[:, 2 * lo:2 * hi], neg_half[:, :, :], mv[:, lo:hi, :],
                                 start=True, stop=True).then_inc(gmean_ps, 1)

            pe.wait_ge(zeros_set, 1)
            for _ in range(WARM):
                nc.tensor.matmul(y_bank[:, :], zeros[:, 0:128], zeros[:, :], start=True, stop=True)
            pe.wait_ge(ident_set, 1)
            pe.wait_ge(wk_in, 32)
            nc.tensor.transpose(pt_bank[0][:, 0:HID], wk[:, :, :], ident[:, :]).then_inc(wkT_ps, 1)
            group_means(0)
            pe.wait_ge(wo_in, 16)
            nc.tensor.transpose(pt_bank[1][:, 0:C], wo[:, :], ident[0:C, 0:C]).then_inc(woT_ps, 1)
            group_means(1)
            for s in range(PAIRS + 4):
                if s < PAIRS:
                    keys(s)
                    transpose_x(s)
                if s < 3:
                    group_means(2 + s)
                if s == 0:
                    pe.wait_ge(woM_set, 1)
                    pe.wait_ge(wv_in, 32)
                    nc.tensor.matmul(chain_bank[:, :], wv[:, :, :], woM[:, :, :], start=True, stop=True).then_inc(g_ps, 1)
                if 0 <= s - 1 < PAIRS:
                    transpose_p(s - 1)
                if 0 <= s - 2 < PAIRS:
                    context(s - 2)
                for g, ps in enumerate(GROUPS):
                    if ps[-1] == s - 2:
                        heads(g)
                        transpose_b(g)
                        project(g)
                        for p in ps:
                            outputs(p)


def kernel(x, L0_conv_w_qkv, L0_conv_w_out, L0_conv_b_out):
    import numpy as np
    import concourse.bacc as bacc
    from concourse.bass_utils import run_bass_kernel_spmd

    nc = bacc.Bacc("TRN2", target_bir_lowering=False, num_devices=1)
    batch, c, h, w = x.shape
    arrays = {
        "x": np.ascontiguousarray(x).reshape(batch, c, h * w),
        "w_qkv": np.ascontiguousarray(L0_conv_w_qkv),
        "w_out": np.ascontiguousarray(L0_conv_w_out),
        "b_out": np.ascontiguousarray(L0_conv_b_out).reshape(c, 1),
    }
    args = [nc.dram_tensor(n, a.shape, mybir.dt.from_np(a.dtype), kind="ExternalInput").ap() for n, a in arrays.items()]
    y = nc.dram_tensor("y", (batch, c, h * w), mybir.dt.float32, kind="ExternalOutput").ap()
    attention_kernel(nc, *args, y)
    r = run_bass_kernel_spmd(nc, [arrays], core_ids=[0])
    return r.results[0]["y"].reshape(batch, c, h, w)
```

```python
import concourse.bass as bass
from concourse import mybir
from contextlib import ExitStack


def attention_kernel(nc, x, w_qkv, w_out, b_out, y):
    F32, BF16 = mybir.dt.float32, mybir.dt.bfloat16
    ALU = mybir.AluOpType
    EXP = mybir.ActivationFunctionType.Exp
    X = mybir.AxisListType.X

    BATCH, C, N = x.shape
    HID = w_out.shape[1]
    HEADS, DH = 8, HID // 8
    PAIRS = BATCH // 2
    CH = N // 128
    EPS = 1e-5
    PER_GROUP = 2

    STATS = [[0], [1], [2, 3], [4, 5], [6, 7]]
    GROUPS = [[0, 1, 2, 3], [4, 5, 6, 7]]
    LOADS = [[0], [1], [2, 3], [4, 5, 6, 7]]
    WARM = [14, 3, 6]

    PE_ORDER = """
        turn_wk0 group_means0 group_means1 turn_wo0 group_means2 keys0 transpose_x0 head_weights0 keys1
        transpose_x1 keys2 transpose_p0 group_means3 transpose_x2 keys3 group_means4 transpose_p1 transpose_p2
        transpose_x3 context0 keys4 keys5 transpose_x4 context1 transpose_p3 transpose_x5 context2 keys6
        context3 keys7 transpose_p4 heads0 transpose_p5 transpose_p6 transpose_x6 context4 transpose_b0
        transpose_p7 context5 transpose_x7 context6 project0 context7 outputs0 heads1 outputs1 transpose_b1
        outputs2 project1 outputs3 outputs4 outputs5 outputs6 outputs7"""
    DVE_ORDER = """
        zero_m0 moments0 aggregate0 moments1 scale_means0 aggregate1 deviation0 variance0 moments2 scale_means1
        aggregate2 deviation1 moments3 variance1 aggregate3 normalise0 scale_means2 deviation2 moments4
        variance2 normalise1 maxima0 normalise2 aggregate4 moments5 normalise3 moments6 maxima1 moments7
        aggregate5 maxima2 scale_means3 aggregate6 deviation3 aggregate7 variance3 maxima3 scale_means4
        normalise4 deviation4 normalise5 variance4 inverse_sums0 normalise6 maxima4 normalise7 maxima5 maxima6
        maxima7 inverse_sums1 scale_b0 copy_m0 residual0 residual1 scale_b1 residual2 copy_m1 residual3
        residual4 residual5 residual6 residual7"""
    ACT_ORDER = """
        copy_wk0 copy_wo0 copy_xt0 exps0 copy_g0 copy_xt1 exps1 copy_pt0 exps2 copy_xt2 copy_pt1 exps3 copy_pt2
        copy_xt3 copy_xt4 exps4 copy_pt3 exps5 copy_xt5 copy_at0 exps6 copy_pt4 exps7 copy_bt0 copy_pt5 copy_xt6
        copy_pt6 copy_pt7 copy_xt7 copy_m0 copy_at1 copy_bt1 copy_m1"""
    POOL_ORDER = """
        inverse_std0 mask_wo0 inverse_std1 inverse_std2 inverse_std3 inverse_std4 inverse_std5 inverse_std6
        inverse_std7"""

    def tasks(order):
        return [(word.rstrip("0123456789"), int(word[len(word.rstrip("0123456789")):])) for word in order.split()]

    group_of = {p: g for g, ps in enumerate(GROUPS) for p in ps}
    load_of = {p: i for i, ps in enumerate(LOADS) for p in ps}

    with ExitStack() as ctx:
        def sb(name, shape, dt=F32):
            return ctx.enter_context(nc.sbuf_tensor(name, shape, dt))

        def bank(name):
            return ctx.enter_context(nc.psum_tensor(name + "_bank", [128, 512], F32))

        def sem(name):
            return ctx.enter_context(nc.semaphore(name))

        ident = sb("ident", [128, 128])
        same_group = sb("same_group", [128, 64, 2])
        head_mask = sb("head_mask", [128, HEADS])
        eps_row = sb("eps_row", [128, 2, 2])
        neg_power = sb("neg_power", [128, 2])
        zeros = sb("zeros", [128, 256], BF16)
        scrap = sb("scrap", [128, 1])
        w_sb = sb("w_sb", [HID, 3, C])
        wq, wk, wv = (w_sb[:, i, :] for i in range(3))
        woT = sb("woT", [HID, C])
        wo = sb("wo", [C, HID])
        bias = sb("bias", [128, 1])
        wkT = sb("wkT", [128, 2, HID])
        woM = sb("woM", [HID, HEADS, C])
        G = sb("G", [128, HEADS, C])
        x_sb = sb("x_sb", [128, PAIRS, N])
        xn = sb("xn", [128, PAIRS, N])
        stats6 = sb("stats6", [128, PAIRS, 6])
        mv = sb("mv", [128, PAIRS, 2])
        gmv = sb("gmv", [128, PAIRS, 2])
        dev = sb("dev", [128, PAIRS])
        var = sb("var", [128, PAIRS])
        rstd = sb("rstd", [128, PAIRS])
        nmax = sb("nmax", [128, BATCH])
        psum_d = sb("psum_d", [128, BATCH])
        rsum = sb("rsum", [128, BATCH])
        P = sb("P", [128, BATCH, N])
        PT = sb("PT", [128, PAIRS, 2, CH, HID])
        xT = sb("xT", [128, PAIRS, CH, 128])
        AT = sb("AT", [128, PAIRS, HID])
        BT = sb("BT", [128, PAIRS, HID])
        B = sb("B", [HID, PAIRS, 2, C])
        MT = sb("MT", [128, PAIRS, 2, C])
        y_sb = sb("y_sb", [128, PAIRS, N])

        k_bank = [bank("k0"), bank("k1")]
        pt_bank = [bank("pt0"), bank("pt1")]
        xt_bank = bank("xt")
        at_bank = bank("at")
        chain_bank = bank("chain")
        y_bank = bank("y")
        y_banks = [y_bank] * GROUPS[-1][0] + [k_bank[0], k_bank[1], y_bank, pt_bank[0]][0:len(GROUPS[-1])]

        x_in = [sem(f"x_in{i}") for i in range(len(LOADS))]
        w_in, wo_in, bias_in = (sem(n) for n in ("w_in", "wo_in", "bias_in"))
        zeros_set, ident_set, same_set, small_set, mask_set, step_set, mt_zero, wk_zero = (
            sem(n) for n in ("zeros_set", "ident_set", "same_set", "small_set", "mask_set", "step_set", "mt_zero",
                             "wk_zero"))
        wkT_ps, wkT_set, woT_ps, woT_set, woM_set, g_ps, g_set = (
            sem(n) for n in ("wkT_ps", "wkT_set", "woT_ps", "woT_set", "woM_set", "g_ps", "g_set"))
        bn_done = sem("bn_done")
        mv_done = sem("mv_done")
        gmean_ps = sem("gmean_ps")
        gmv_done = sem("gmv_done")
        dev_done = sem("dev_done")
        var_done = sem("var_done")
        rstd_done = sem("rstd_done")
        xn_done = sem("xn_done")
        k_ps = sem("k_ps")
        max_done = sem("max_done")
        exp_done = sem("exp_done")
        xt_ps = sem("xt_ps")
        xt_done = sem("xt_done")
        pt_ps = sem("pt_ps")
        pt_done = sem("pt_done")
        at_ps = sem("at_ps")
        at_done = sem("at_done")
        bt_ps = sem("bt_ps")
        bt_done = sem("bt_done")
        rsum_done = sem("rsum_done")
        b_ps = sem("b_ps")
        b_done = sem("b_done")
        m_ps = sem("m_ps")
        m_done = [sem("m_done0"), sem("m_done1")]
        y_ps = sem("y_ps")
        y_done = sem("y_done")
        y_out = sem("y_out")

        x_v = x.rearrange("(p two) c n -> (two c) p n", two=2)
        y_v = y.rearrange("(p two) c n -> (two c) p n", two=2)

        block = ctx.enter_context(nc.Block())

        @block.sync
        def _(sp):
            def load_x(i):
                lo, hi = LOADS[i][0], LOADS[i][-1] + 1
                sp.dma_start(x_sb[:, lo:hi, :], x_v[:, lo:hi, :]).then_inc(x_in[i], 16)

            load_x(0)
            sp.dma_start(w_sb[:, :, :], w_qkv.rearrange("(t d) c -> d t c", t=3)).then_inc(w_in, 16)
            load_x(1)
            load_x(2)
            sp.dma_start(wo[:, :], w_out).then_inc(wo_in, 16)
            load_x(3)
            for half in range(2):
                sp.dma_start(bias[C * half:C * half + C, :], b_out).then_inc(bias_in, 16)
            for p in range(PAIRS):
                sp.wait_ge(y_done, p + 1)
                sp.dma_start(y_v[:, p, :], y_sb[:, p, :]).then_inc(y_out, 16)
            sp.wait_ge(y_out, 16 * PAIRS)

        @block.gpsimd
        def _(pool):
            def keep(tile, op, fill, base, mult, pattern):
                return nc.gpsimd.affine_select(out=tile, in_=tile, compare_op=op, fill=fill, base=base,
                                               pattern=pattern, channel_multiplier=mult)

            nc.gpsimd.memset(ident[:, :], 0.0).then_inc(step_set, 1)
            pool.wait_ge(step_set, 1)
            keep(ident[:, :], ALU.not_equal, 1.0, 0, 1, [[-1, 128]]).then_inc(ident_set, 1)
            nc.gpsimd.memset(head_mask[:, :], 1.0).then_inc(step_set, 1)
            pool.wait_ge(step_set, 2)
            keep(head_mask[:, :], ALU.is_ge, 0.0, 0, 1, [[-DH, HEADS]]).then_inc(step_set, 1)
            pool.wait_ge(step_set, 3)
            keep(head_mask[:, :], ALU.is_ge, 0.0, DH - 1, -1, [[DH, HEADS]]).then_inc(mask_set, 1)

            def inverse_std(p):
                pool.wait_ge(var_done, p + 1)
                nc.gpsimd.tensor_tensor(rstd[:, p:p + 1], var[:, p:p + 1], neg_power[:, 0:1],
                                        ALU.pow).then_inc(rstd_done, 1)

            def mask_wo(_):
                pool.wait_ge(woT_set, 1)
                pool.wait_ge(mask_set, 1)
                nc.gpsimd.tensor_tensor(woM[:, :, :], woT[:, :].unsqueeze(1).to_broadcast([128, HEADS, C]),
                                        head_mask[:, :].unsqueeze(2).to_broadcast([128, HEADS, C]),
                                        ALU.mult).then_inc(woM_set, 1)

            pool.wait_ge(small_set, 1)
            run = {"inverse_std": inverse_std, "mask_wo": mask_wo}
            for task, i in tasks(POOL_ORDER):
                run[task](i)

        @block.scalar
        def _(act):
            act.wait_ge(zeros_set, 1)
            nc.scalar.activation(scrap[:, :], zeros[:, 0:1], EXP)

            def copy_wk(_):
                act.wait_ge(wkT_ps, 1)
                act.wait_ge(wk_zero, 1)
                for half in range(2):
                    nc.scalar.copy(wkT[C * half:C * half + C, half, :], pt_bank[0][0:C, 0:HID]).then_inc(wkT_set, 1)

            def copy_wo(_):
                act.wait_ge(woT_ps, 1)
                nc.scalar.copy(woT[:, :], pt_bank[1][:, 0:C]).then_inc(woT_set, 1)

            def copy_g(_):
                act.wait_ge(g_ps, 1)
                nc.scalar.copy(G[:, :, :], chain_bank[:, :]).then_inc(g_set, 1)

            def exps(p):
                act.wait_ge(max_done, p + 1)
                for half in range(2):
                    b = 2 * p + half
                    nc.scalar.activation(P[:, b, :], k_bank[p % 2][:, half * N:(half + 1) * N], EXP,
                                         bias=nmax[:, b:b + 1], accum_out=psum_d[:, b:b + 1]).then_inc(exp_done, 1)

            def copy_pt(p):
                act.wait_ge(pt_ps, p + 1)
                nc.scalar.copy(PT[:, p, :, :, :], pt_bank[p % 2][:, :]).then_inc(pt_done, 1)

            def copy_xt(p):
                act.wait_ge(xt_ps, p + 1)
                nc.scalar.copy(xT[:, p, :, :], xt_bank[:, 0:CH * 128]).then_inc(xt_done, 1)

            def copy_m(g):
                half, ps = 1, GROUPS[g]
                rows = slice(C * half, C * half + C)
                act.wait_ge(m_ps, g + 1)
                act.wait_ge(mt_zero, 1)
                nc.scalar.copy(MT[rows, ps[0]:ps[-1] + 1, half, :],
                               chain_bank[rows, 0:len(ps) * C]).then_inc(m_done[half], 1)

            def copy_at(g):
                ps = GROUPS[g]
                act.wait_ge(at_ps, ps[-1] + 1)
                nc.scalar.copy(AT[:, ps[0]:ps[-1] + 1, :], at_bank[:, 0:len(ps) * HID]).then_inc(at_done, 1)

            def copy_bt(g):
                ps = GROUPS[g]
                act.wait_ge(bt_ps, g + 1)
                nc.scalar.copy(BT[:, ps[0]:ps[-1] + 1, :], chain_bank[:, 0:len(ps) * HID]).then_inc(bt_done, 1)

            run = {"copy_wk": copy_wk, "copy_wo": copy_wo, "copy_g": copy_g, "copy_xt": copy_xt, "exps": exps,
                   "copy_pt": copy_pt, "copy_at": copy_at, "copy_bt": copy_bt, "copy_m": copy_m}
            for task, i in tasks(ACT_ORDER):
                run[task](i)

        @block.vector
        def _(dve):
            def moments(p):
                dve.wait_ge(x_in[load_of[p]], 16)
                nc.vector.bn_stats(stats6[:, p, :], x_sb[:, p, :]).then_inc(bn_done, 1)

            def aggregate(p):
                dve.wait_ge(bn_done, p + 1)
                nc.vector.bn_aggr(mv[:, p, :], stats6[:, p, :]).then_inc(mv_done, 1)

            def scale_means(i):
                ps = STATS[i]
                lo, hi = ps[0], ps[-1] + 1
                dve.wait_ge(gmean_ps, i + 1)
                nc.vector.scalar_tensor_tensor(gmv[:, lo:hi, :], at_bank[:, 2 * lo:2 * hi], -1.0 / PER_GROUP,
                                               eps_row[:, 0:hi - lo, :], ALU.mult, ALU.add).then_inc(gmv_done, 1)

            def deviation(i):
                ps = STATS[i]
                lo, hi = ps[0], ps[-1] + 1
                dve.wait_ge(gmv_done, i + 1)
                nc.vector.tensor_tensor(dev[:, lo:hi], mv[:, lo:hi, 0], gmv[:, lo:hi, 0],
                                        ALU.add).then_inc(dev_done, 1)

            def variance(i):
                dve.wait_ge(dev_done, i + 1)
                for p in STATS[i]:
                    nc.vector.scalar_tensor_tensor(var[:, p:p + 1], dev[:, p:p + 1], dev[:, p:p + 1], gmv[:, p, 1:2],
                                                   ALU.mult, ALU.subtract).then_inc(var_done, 1)

            def normalise(p):
                dve.wait_ge(rstd_done, p + 1)
                nc.vector.tensor_scalar(xn[:, p, :], x_sb[:, p, :], gmv[:, p, 0:1], rstd[:, p:p + 1],
                                        ALU.add, ALU.mult).then_inc(xn_done, 1)

            def maxima(p):
                dve.wait_ge(k_ps, p + 1)
                nc.vector.tensor_reduce(nmax[:, 2 * p:2 * p + 2], k_bank[p % 2][:, :].rearrange("d (h n) -> d h n", h=2),
                                        X, ALU.max, negate=True).then_inc(max_done, 1)

            def inverse_sums(g):
                lo, hi = 2 * GROUPS[g][0], 2 * GROUPS[g][-1] + 2
                dve.wait_ge(exp_done, hi)
                nc.vector.reciprocal(rsum[:, lo:hi], psum_d[:, lo:hi]).then_inc(rsum_done, 1)

            def scale_b(g):
                ps = GROUPS[g]
                n = 2 * len(ps)
                dve.wait_ge(b_ps, g + 1)
                dve.wait_ge(rsum_done, g + 1)
                nc.vector.tensor_tensor(B[:, ps[0]:ps[-1] + 1, :, :].rearrange("d p h o -> d (p h) o"),
                                        chain_bank[:, 0:n * C].rearrange("d (b o) -> d b o", b=n),
                                        rsum[:, 2 * ps[0]:2 * ps[0] + n].unsqueeze(2).to_broadcast([128, n, C]),
                                        ALU.mult).then_inc(b_done, 1)

            def copy_m(g):
                half, ps = 0, GROUPS[g]
                rows = slice(C * half, C * half + C)
                dve.wait_ge(m_ps, g + 1)
                dve.wait_ge(mt_zero, 1)
                nc.vector.tensor_copy(MT[rows, ps[0]:ps[-1] + 1, half, :],
                                      chain_bank[rows, 0:len(ps) * C]).then_inc(m_done[half], 1)

            def residual(p):
                dve.wait_ge(y_ps, p + 1)
                if p == 0:
                    dve.wait_ge(bias_in, 32)
                nc.vector.scalar_tensor_tensor(y_sb[:, p, :], y_banks[p][:, 0:N], bias[:, :], x_sb[:, p, :],
                                               ALU.add, ALU.add).then_inc(y_done, 1)

            nc.vector.memset(zeros[:, :], 0.0).then_inc(zeros_set, 1)
            nc.vector.memset(wkT[:, :, :], 0.0).then_inc(wk_zero, 1)
            nc.vector.memset(neg_power[:, :], -0.5).then_inc(small_set, 1)
            nc.vector.memset(eps_row[:, :, 0], 0.0).then_inc(small_set, 1)
            nc.vector.memset(eps_row[:, :, 1], -EPS).then_inc(small_set, 1)
            dve.wait_ge(ident_set, 1)
            columns = ident[:, :].rearrange("p (g j) -> p g j", j=PER_GROUP)
            nc.vector.tensor_tensor(same_group[:, :, :], columns[:, :, 0:1].to_broadcast([128, 64, PER_GROUP]),
                                    columns[:, :, 1:2].to_broadcast([128, 64, PER_GROUP]), ALU.add).then_inc(same_set, 1)
            dve.wait_ge(small_set, 3)

            def zero_m(_):
                nc.vector.memset(MT[:, :, :, :], 0.0).then_inc(mt_zero, 1)

            run = {"zero_m": zero_m, "moments": moments, "aggregate": aggregate, "scale_means": scale_means,
                   "deviation": deviation, "variance": variance, "normalise": normalise, "maxima": maxima,
                   "inverse_sums": inverse_sums, "scale_b": scale_b, "copy_m": copy_m, "residual": residual}
            for task, i in tasks(DVE_ORDER):
                run[task](i)

        @block.tensor
        def _(pe):
            def warm(n):
                for _ in range(n):
                    nc.tensor.matmul(y_bank[:, 0:256], zeros[:, 0:128], zeros[:, :], start=True, stop=True)

            def transpose_x(p):
                pe.wait_ge(xn_done, p + 1)
                if p >= 1:
                    pe.wait_ge(xt_done, p)
                for ch in range(CH):
                    last = nc.tensor.transpose(xt_bank[:, ch * 128:(ch + 1) * 128],
                                               xn[:, p, ch * 128:(ch + 1) * 128], ident[:, :])
                last.then_inc(xt_ps, 1)

            def keys(p):
                pe.wait_ge(xn_done, p + 1)
                if p == 0:
                    pe.wait_ge(wkT_set, 2)
                if p >= 2:
                    pe.wait_ge(exp_done, 2 * (p - 1))
                for half in range(2):
                    last = nc.tensor.matmul(k_bank[p % 2][:, half * N:(half + 1) * N], wkT[:, half, :], xn[:, p, :],
                                            start=True, stop=True)
                last.then_inc(k_ps, 1)

            def transpose_p(p):
                pe.wait_ge(exp_done, 2 * p + 2)
                if p == 1:
                    pe.wait_ge(woT_set, 1)
                if p >= 2:
                    pe.wait_ge(pt_done, p - 1)
                for half in range(2):
                    for ch in range(CH):
                        c0 = (half * CH + ch) * 128
                        last = nc.tensor.transpose(pt_bank[p % 2][:, c0:c0 + 128],
                                                   P[:, 2 * p + half, ch * 128:(ch + 1) * 128], ident[:, :])
                last.then_inc(pt_ps, 1)

            def context(p):
                g = group_of[p]
                pe.wait_ge(pt_done, p + 1)
                pe.wait_ge(xt_done, p + 1)
                if p == 0:
                    pe.wait_ge(gmv_done, len(STATS))
                elif p == GROUPS[g][0]:
                    pe.wait_ge(at_done, g)
                c0 = (p - GROUPS[g][0]) * HID
                for ch in range(CH):
                    for half in range(2):
                        rows = slice(C * half, C * half + C)
                        last = nc.tensor.matmul(at_bank[rows, c0:c0 + HID], xT[:, p, ch, rows], PT[:, p, half, ch, :],
                                                start=(ch == 0), stop=(ch == CH - 1))
                last.then_inc(at_ps, 1)

            def heads(g):
                ps = GROUPS[g]
                pe.wait_ge(at_done, g + 1)
                if g == 0:
                    pe.wait_ge(g_set, 1)
                else:
                    for half in range(2):
                        pe.wait_ge(m_done[half], g)
                out = chain_bank[:, 0:len(ps) * HID].rearrange("o (p d) -> o p d", p=len(ps))
                for h in range(HEADS):
                    for half in range(2):
                        rows = slice(C * half, C * half + C)
                        last = nc.tensor.matmul(out[rows, :, h * DH:(h + 1) * DH], G[rows, h, :],
                                                AT[rows, ps[0]:ps[-1] + 1, h * DH:(h + 1) * DH],
                                                start=True, stop=True)
                last.then_inc(bt_ps, 1)

            def transpose_b(g):
                pe.wait_ge(bt_done, g + 1)
                for i, p in enumerate(GROUPS[g]):
                    last = nc.tensor.transpose(chain_bank[:, i * 128:(i + 1) * 128], BT[:, p, :], ident[:, :])
                last.then_inc(b_ps, 1)

            def project(g):
                ps = GROUPS[g]
                pe.wait_ge(b_done, g + 1)
                if g == 0:
                    pe.wait_ge(w_in, 16)
                for half in range(2):
                    last = nc.tensor.matmul(chain_bank[C * half:C * half + C, 0:len(ps) * C], wq,
                                            B[:, ps[0]:ps[-1] + 1, half, :], start=True, stop=True)
                last.then_inc(m_ps, 1)

            def outputs(p):
                g = group_of[p]
                for half in range(2):
                    pe.wait_ge(m_done[half], g + 1)
                earlier = [q for q in range(p) if y_banks[q] is y_banks[p]]
                if earlier:
                    pe.wait_ge(y_done, earlier[-1] + 1)
                if y_banks[p] in k_bank:
                    pe.wait_ge(exp_done, BATCH)
                if y_banks[p] in pt_bank:
                    pe.wait_ge(pt_done, PAIRS)
                nc.tensor.matmul(y_banks[p][:, 0:N], MT[:, p, :, :], xn[:, p, :],
                                 start=True, stop=True).then_inc(y_ps, 1)

            def group_means(i):
                ps = STATS[i]
                lo, hi = ps[0], ps[-1] + 1
                pe.wait_ge(mv_done, hi)
                if i == 0:
                    pe.wait_ge(same_set, 1)
                else:
                    pe.wait_ge(gmv_done, i)
                nc.tensor.matmul(at_bank[:, 2 * lo:2 * hi], same_group[:, :, :], mv[:, lo:hi, :],
                                 start=True, stop=True).then_inc(gmean_ps, 1)
                if i == 0:
                    warm(WARM[1])

            def turn_wk(_):
                pe.wait_ge(ident_set, 1)
                pe.wait_ge(w_in, 16)
                nc.tensor.transpose(pt_bank[0][0:C, 0:HID], wk, ident[:, :]).then_inc(wkT_ps, 1)

            def turn_wo(_):
                pe.wait_ge(wo_in, 16)
                nc.tensor.transpose(pt_bank[1][:, 0:C], wo[:, :], ident[0:C, 0:C]).then_inc(woT_ps, 1)
                warm(WARM[2])

            def head_weights(_):
                pe.wait_ge(woM_set, 1)
                for half in range(2):
                    last = nc.tensor.matmul(chain_bank[C * half:C * half + C, :], wv, woM[:, :, :],
                                            start=True, stop=True)
                last.then_inc(g_ps, 1)

            pe.wait_ge(zeros_set, 1)
            warm(WARM[0])
            run = {"turn_wk": turn_wk, "turn_wo": turn_wo, "group_means": group_means, "head_weights": head_weights,
                   "keys": keys, "transpose_x": transpose_x, "transpose_p": transpose_p, "context": context,
                   "heads": heads, "transpose_b": transpose_b, "project": project, "outputs": outputs}
            for task, i in tasks(PE_ORDER):
                run[task](i)


def kernel(x, L0_conv_w_qkv, L0_conv_w_out, L0_conv_b_out):
    import numpy as np
    import concourse.bacc as bacc
    from concourse.bass_utils import run_bass_kernel_spmd

    nc = bacc.Bacc("TRN2", target_bir_lowering=False, num_devices=1)
    batch, c, h, w = x.shape
    arrays = {
        "x": np.ascontiguousarray(x).reshape(batch, c, h * w),
        "w_qkv": np.ascontiguousarray(L0_conv_w_qkv),
        "w_out": np.ascontiguousarray(L0_conv_w_out),
        "b_out": np.ascontiguousarray(L0_conv_b_out).reshape(c, 1),
    }
    args = [nc.dram_tensor(n, a.shape, mybir.dt.from_np(a.dtype), kind="ExternalInput").ap() for n, a in arrays.items()]
    y = nc.dram_tensor("y", (batch, c, h * w), mybir.dt.float32, kind="ExternalOutput").ap()
    attention_kernel(nc, *args, y)
    r = run_bass_kernel_spmd(nc, [arrays], core_ids=[0])
    return r.results[0]["y"].reshape(batch, c, h, w)
```

```python
import concourse.bass as bass
from concourse import mybir
from contextlib import ExitStack


def attention_kernel(nc, x, w_qkv, w_out, b_out, y):
    F32, F32R, BF16 = mybir.dt.float32, mybir.dt.float32r, mybir.dt.bfloat16
    ALU = mybir.AluOpType
    EXP = mybir.ActivationFunctionType.Exp
    X = mybir.AxisListType.X

    BATCH, C, N = x.shape
    HID = w_out.shape[1]
    HEADS, DH = 8, HID // 8
    PAIRS = BATCH // 2
    BLOCK, BLOCKS = 32, HID // 32
    CH = N // 128
    EPS = 1e-5
    PER_GROUP = 2

    STATS = [[0], [1], [2, 3], [4, 5], [6, 7]]
    GROUPS = [[0, 1], [2, 3], [4, 5], [6, 7]]
    LOADS = [[0], [1], [2, 3], [4, 5], [6, 7]]
    WHOLE = 3
    WARM = {("group_means", 0): 13, ("turn_wk", 0): 2, ("group_means", 2): 8}

    PE_ORDER = """
        group_means0 turn_wk0 group_means1 group_means2 turn_wo0 transpose_x0 keys0 transpose_x1 turn_wv0 keys1
        group_means3 transpose_x2 keys2 transpose_p0 transpose_x3 group_means4 transpose_p1 keys3 context0
        context1 transpose_x4 transpose_p2 values0 transpose_x5 keys4 transpose_p3 transpose_x6 mix0 context2
        keys5 context3 project0 transpose_x7 keys6 transpose_p4 outputs0 values1 transpose_p5 keys7 context4
        mix1 context5 transpose_p6 transpose_p7 project1 values2 context6 context7 mix2 values3 outputs1
        project2 mix3 outputs2 outputs3 project3 outputs4 outputs5 outputs6 outputs7"""
    DVE_ORDER = """
        moments0 aggregate0 moments1 scale_means0 aggregate1 deviation0 variance0 moments2 scale_means1
        aggregate2 deviation1 moments3 variance1 aggregate3 moments4 normalise0 moments5 scale_means2 normalise1
        deviation2 aggregate4 variance2 moments6 maxima0 aggregate5 normalise2 normalise3 maxima1 split_wk0
        aggregate6 scale_means3 moments7 deviation3 aggregate7 variance3 split_low_b3 scale_means4 maxima2
        deviation4 normalise4 variance4 split_high4 maxima3 normalise5 split_low_a4 inverse_sums0 split_high5
        normalise6 mask_v0 split_low_b5 maxima4 split_high6 normalise7 split_low_a6 scale_b0 maxima5
        split_low_b7 copy_m0 maxima6 mask_v1 inverse_sums1 copy_xt7 maxima7 inverse_sums2 scale_b1 inverse_sums3
        copy_pt7 mask_v2 copy_m1 residual0 scale_b2 mask_v3 residual1 copy_m2 scale_b3 residual2 residual3
        copy_m3 residual4 residual5 residual6 residual7"""
    ACT_ORDER = """
        copy_wk0 copy_wk_high0 copy_wo0 copy_xt0 copy_xt1 copy_wv0 exps0 split_high3 copy_xt2 exps1 copy_pt0
        copy_xt3 copy_pt1 exps2 copy_at0 copy_xt4 exps3 copy_xt5 copy_pt2 copy_pt3 exps4 copy_xt6 split_high7
        copy_m0 copy_at1 exps5 copy_pt4 exps6 copy_pt5 exps7 copy_at2 copy_pt6 copy_m1 copy_at3 copy_m2 copy_m3"""
    POOL_ORDER = """
        inverse_std0 inverse_std1 inverse_std2 inverse_std3 split_low_a3 inverse_std4 inverse_std5 inverse_std6
        split_low_b4 split_low_a5 inverse_std7 split_low_b6 split_low_a7"""

    def tasks(order):
        return [(word.rstrip("0123456789"), int(word[len(word.rstrip("0123456789")):])) for word in order.split()]

    group_of = {p: g for g, ps in enumerate(GROUPS) for p in ps}
    load_of = {p: i for i, ps in enumerate(LOADS) for p in ps}

    with ExitStack() as ctx:
        def sb(name, shape, dt=F32):
            return ctx.enter_context(nc.sbuf_tensor(name, shape, dt))

        def bank(name):
            return ctx.enter_context(nc.psum_tensor(name + "_bank", [128, 512], F32))

        def sem(name):
            return ctx.enter_context(nc.semaphore(name))

        ident = sb("ident", [128, 128])
        same_group = sb("same_group", [128, 64, 2])
        head_mask = sb("head_mask", [128, HEADS])
        block_mask = sb("block_mask", [128, BLOCK // DH])
        eps_row = sb("eps_row", [128, 2, 2])
        neg_power = sb("neg_power", [128, 2])
        zeros = sb("zeros", [128, 256], BF16)
        scrap = sb("scrap", [128, 1])
        w_sb = sb("w_sb", [HID, 3, C])
        wq, wk, wv = (w_sb[:, i, :] for i in range(3))
        woT = sb("woT", [HID, C])
        wo = sb("wo", [C, HID])
        bias = sb("bias", [128, 1])
        wkT = sb("wkT", [128, 2, HID])
        wvT = sb("wvT", [128, 2, HID])
        wk_high = sb("wk_high", [128, HID], F32R)
        wk_low = sb("wk_low", [128, HID], F32R)
        x_sb = sb("x_sb", [128, PAIRS, N])
        xn = sb("xn", [128, PAIRS, N])
        stats6 = sb("stats6", [128, PAIRS, 6])
        mv = sb("mv", [128, PAIRS, 2])
        gmv = sb("gmv", [128, PAIRS, 2])
        dev = sb("dev", [128, PAIRS])
        var = sb("var", [128, PAIRS])
        rstd = sb("rstd", [128, PAIRS])
        nmax = sb("nmax", [128, BATCH])
        psum_d = sb("psum_d", [128, BATCH])
        rsum = sb("rsum", [128, BATCH])
        P = sb("P", [128, BATCH, N])
        PT = sb("PT", [128, PAIRS, 2, CH, HID])
        xT = sb("xT", [128, PAIRS, CH, 128])
        AT = sb("AT", [128, PAIRS, HID])
        V = sb("V", [HID, BATCH, BLOCK])
        parts = sb("parts", [128, PAIRS, 2, N], F32R)
        B = sb("B", [HID, PAIRS, 2, C])
        MT = sb("MT", [128, PAIRS, 2, C])
        y_sb = sb("y_sb", [128, PAIRS, N])

        k_bank = [bank("k0"), bank("k1")]
        pt_bank = [bank("pt0"), bank("pt1")]
        xt_bank = bank("xt")
        at_bank = bank("at")
        chain_bank = bank("chain")
        y_bank = bank("y")
        chain_banks = [chain_bank, chain_bank, xt_bank, k_bank[0]]
        y_banks = [y_bank, y_bank, y_bank, chain_bank, k_bank[1], y_bank, pt_bank[0], pt_bank[1]]

        x_in = [sem(f"x_in{i}") for i in range(len(LOADS))]
        w_in, wo_in, bias_in = (sem(n) for n in ("w_in", "wo_in", "bias_in"))
        zeros_set, ident_set, same_set, small_set, mask_set, step_set, block_set, mt_zero, pad_zero = (
            sem(n) for n in ("zeros_set", "ident_set", "same_set", "small_set", "mask_set", "step_set", "block_set",
                             "mt_zero",
                             "pad_zero"))
        wkT_ps, wkT_set, wk_high_set, wk_low_set, wvT_ps, wvT_set, woT_ps, woT_set = (
            sem(n) for n in ("wkT_ps", "wkT_set", "wk_high_set", "wk_low_set", "wvT_ps", "wvT_set", "woT_ps", "woT_set"))
        bn_done = sem("bn_done")
        mv_done = sem("mv_done")
        gmean_ps = sem("gmean_ps")
        gmv_done = sem("gmv_done")
        dev_done = sem("dev_done")
        var_done = sem("var_done")
        rstd_done = sem("rstd_done")
        xn_done = sem("xn_done")
        k_ps = sem("k_ps")
        max_done = sem("max_done")
        exp_done = sem("exp_done")
        xt_ps = sem("xt_ps")
        pt_ps = sem("pt_ps")
        at_ps = sem("at_ps")
        at_done = sem("at_done")
        v_ps = sem("v_ps")
        v_done = sem("v_done")
        rsum_done = sem("rsum_done")
        b_ps = sem("b_ps")
        b_done = sem("b_done")
        m_ps = sem("m_ps")
        m_done = [sem("m_done0"), sem("m_done1")]
        y_ps = sem("y_ps")
        y_done = sem("y_done")
        y_out = sem("y_out")
        SHARED = {"copy_xt": ("act", "dve"), "copy_pt": ("act", "dve"), "split_high": ("act", "dve"),
                  "split_low_a": ("dve", "pool"), "split_low_b": ("dve", "pool")}
        shared_done = {(task, who): sem(f"{task}_{who}") for task, pair in SHARED.items() for who in pair}
        ORDERS = {"act": tasks(ACT_ORDER), "dve": tasks(DVE_ORDER), "pool": tasks(POOL_ORDER)}

        def wait_shared(engine, task, i):
            for who in SHARED[task]:
                if (task, i) in ORDERS[who]:
                    at = ORDERS[who].index((task, i))
                    engine.wait_ge(shared_done[task, who], sum(t == task for t, _ in ORDERS[who][:at + 1]))

        x_v = x.rearrange("(p two) c n -> (two c) p n", two=2)
        y_v = y.rearrange("(p two) c n -> (two c) p n", two=2)

        block = ctx.enter_context(nc.Block())

        @block.sync
        def _(sp):
            def load_x(i):
                lo, hi = LOADS[i][0], LOADS[i][-1] + 1
                sp.dma_start(x_sb[:, lo:hi, :], x_v[:, lo:hi, :]).then_inc(x_in[i], 16)

            load_x(0)
            sp.dma_start(w_sb[:, :, :], w_qkv.rearrange("(t d) c -> d t c", t=3)).then_inc(w_in, 16)
            load_x(1)
            load_x(2)
            sp.dma_start(wo[:, :], w_out).then_inc(wo_in, 16)
            load_x(3)
            load_x(4)
            for half in range(2):
                sp.dma_start(bias[C * half:C * half + C, :], b_out).then_inc(bias_in, 16)
            for p in range(PAIRS):
                sp.wait_ge(y_done, p + 1)
                sp.dma_start(y_v[:, p, :], y_sb[:, p, :]).then_inc(y_out, 16)
            sp.wait_ge(y_out, 16 * PAIRS)

        def low_part(engine, ops, p, half):
            wait_shared(engine, "split_high", p)
            rows, other = slice(C * half, C * half + C), slice(C * (1 - half), C * (1 - half) + C)
            return ops.tensor_tensor(parts[other, p, half, :], xn[rows, p, :], parts[rows, p, half, :].bitcast(F32),
                                     ALU.subtract)

        @block.gpsimd
        def _(pool):
            def keep(tile, op, fill, base, mult, pattern):
                return nc.gpsimd.affine_select(out=tile, in_=tile, compare_op=op, fill=fill, base=base,
                                               pattern=pattern, channel_multiplier=mult)

            nc.gpsimd.memset(ident[:, :], 0.0).then_inc(step_set, 1)
            pool.wait_ge(step_set, 1)
            keep(ident[:, :], ALU.not_equal, 1.0, 0, 1, [[-1, 128]]).then_inc(ident_set, 1)
            nc.gpsimd.memset(head_mask[:, :], 1.0).then_inc(step_set, 1)
            pool.wait_ge(step_set, 2)
            keep(head_mask[:, :], ALU.is_ge, 0.0, 0, 1, [[-DH, HEADS]]).then_inc(step_set, 1)
            pool.wait_ge(step_set, 3)
            keep(head_mask[:, :], ALU.is_ge, 0.0, DH - 1, -1, [[DH, HEADS]]).then_inc(mask_set, 1)

            nc.gpsimd.memset(MT[:, :, :, :], 0.0).then_inc(mt_zero, 1)

            def inverse_std(p):
                pool.wait_ge(var_done, p + 1)
                nc.gpsimd.tensor_tensor(rstd[:, p:p + 1], var[:, p:p + 1], neg_power[:, 0:1],
                                        ALU.pow).then_inc(rstd_done, 1)

            def split_low(task, p, half):
                powers = sum(t == "inverse_std" for t, _ in ORDERS["pool"][:ORDERS["pool"].index((task, p))])
                if powers:
                    pool.wait_ge(rstd_done, powers)
                low_part(pool, nc.gpsimd, p, half).then_inc(shared_done[task, "pool"], 1)
                wait_shared(pool, task, p)

            pool.wait_ge(small_set, 1)
            run = {"inverse_std": inverse_std,
                   "split_low_a": lambda p: split_low("split_low_a", p, 0),
                   "split_low_b": lambda p: split_low("split_low_b", p, 1)}
            for task, i in tasks(POOL_ORDER):
                run[task](i)

        @block.scalar
        def _(act):
            act.wait_ge(zeros_set, 1)
            nc.scalar.activation(scrap[:, :], zeros[:, 0:1], EXP)

            def copy_wk(_):
                act.wait_ge(wkT_ps, 1)
                act.wait_ge(pad_zero, 2)
                for half in range(2):
                    nc.scalar.copy(wkT[C * half:C * half + C, half, :], pt_bank[0][0:C, 0:HID]).then_inc(wkT_set, 1)

            def copy_wk_high(_):
                act.wait_ge(wkT_ps, 1)
                for half in range(2):
                    nc.scalar.copy(wk_high[C * half:C * half + C, :], pt_bank[0][0:C, 0:HID]).then_inc(wk_high_set, 1)

            def copy_wv(_):
                act.wait_ge(wvT_ps, 1)
                act.wait_ge(pad_zero, 2)
                for half in range(2):
                    nc.scalar.copy(wvT[C * half:C * half + C, half, :], chain_bank[0:C, 0:HID]).then_inc(wvT_set, 1)

            def copy_wo(_):
                act.wait_ge(woT_ps, 1)
                nc.scalar.copy(woT[:, :], pt_bank[1][:, 0:C]).then_inc(woT_set, 1)

            def exps(p):
                act.wait_ge(max_done, p + 1)
                for half in range(2):
                    b = 2 * p + half
                    nc.scalar.activation(P[:, b, :], k_bank[p % 2][:, half * N:(half + 1) * N], EXP,
                                         bias=nmax[:, b:b + 1], accum_out=psum_d[:, b:b + 1]).then_inc(exp_done, 1)

            def copy_pt(p):
                act.wait_ge(pt_ps, p + 1)
                nc.scalar.copy(PT[:, p, :, :, :], pt_bank[p % 2][:, :]).then_inc(shared_done["copy_pt", "act"], 1)

            def copy_xt(p):
                act.wait_ge(xt_ps, p + 1)
                nc.scalar.copy(xT[:, p, :, :], xt_bank[:, 0:CH * 128]).then_inc(shared_done["copy_xt", "act"], 1)

            def split_high(p):
                act.wait_ge(xn_done, p + 1)
                nc.scalar.copy(parts[:, p, :, :], xn[:, p:p + 1, :].to_broadcast([128, 2, N])).then_inc(
                    shared_done["split_high", "act"], 1)

            def copy_m(g):
                half, ps = 1, GROUPS[g]
                rows = slice(C * half, C * half + C)
                act.wait_ge(m_ps, g + 1)
                act.wait_ge(mt_zero, 1)
                nc.scalar.copy(MT[rows, ps[0]:ps[-1] + 1, half, :],
                               chain_banks[g][rows, 0:len(ps) * C]).then_inc(m_done[half], 1)

            def copy_at(g):
                ps = GROUPS[g]
                act.wait_ge(at_ps, ps[-1] + 1)
                nc.scalar.copy(AT[:, ps[0]:ps[-1] + 1, :], at_bank[:, 0:len(ps) * HID]).then_inc(at_done, 1)

            run = {"copy_wk": copy_wk, "copy_wk_high": copy_wk_high, "copy_wv": copy_wv, "copy_wo": copy_wo,
                   "copy_xt": copy_xt, "split_high": split_high, "exps": exps, "copy_pt": copy_pt,
                   "copy_at": copy_at, "copy_m": copy_m}
            for task, i in tasks(ACT_ORDER):
                run[task](i)

        @block.vector
        def _(dve):
            def moments(p):
                dve.wait_ge(x_in[load_of[p]], 16)
                nc.vector.bn_stats(stats6[:, p, :], x_sb[:, p, :]).then_inc(bn_done, 1)

            def aggregate(p):
                dve.wait_ge(bn_done, p + 1)
                nc.vector.bn_aggr(mv[:, p, :], stats6[:, p, :]).then_inc(mv_done, 1)

            def scale_means(i):
                ps = STATS[i]
                lo, hi = ps[0], ps[-1] + 1
                dve.wait_ge(gmean_ps, i + 1)
                nc.vector.scalar_tensor_tensor(gmv[:, lo:hi, :], at_bank[:, 2 * lo:2 * hi], -1.0 / PER_GROUP,
                                               eps_row[:, 0:hi - lo, :], ALU.mult, ALU.add).then_inc(gmv_done, 1)

            def deviation(i):
                ps = STATS[i]
                lo, hi = ps[0], ps[-1] + 1
                dve.wait_ge(gmv_done, i + 1)
                nc.vector.tensor_tensor(dev[:, lo:hi], mv[:, lo:hi, 0], gmv[:, lo:hi, 0],
                                        ALU.add).then_inc(dev_done, 1)

            def variance(i):
                dve.wait_ge(dev_done, i + 1)
                for p in STATS[i]:
                    nc.vector.scalar_tensor_tensor(var[:, p:p + 1], dev[:, p:p + 1], dev[:, p:p + 1], gmv[:, p, 1:2],
                                                   ALU.mult, ALU.subtract).then_inc(var_done, 1)

            def normalise(p):
                dve.wait_ge(rstd_done, p + 1)
                nc.vector.tensor_scalar(xn[:, p, :], x_sb[:, p, :], gmv[:, p, 0:1], rstd[:, p:p + 1],
                                        ALU.add, ALU.mult).then_inc(xn_done, 1)

            def maxima(p):
                dve.wait_ge(k_ps, p + 1)
                nc.vector.tensor_reduce(nmax[:, 2 * p:2 * p + 2], k_bank[p % 2][:, :].rearrange("d (h n) -> d h n", h=2),
                                        X, ALU.max, negate=True).then_inc(max_done, 1)

            def copy_pt(p):
                dve.wait_ge(pt_ps, p + 1)
                nc.vector.tensor_copy(PT[:, p, :, :, :], pt_bank[p % 2][:, :]).then_inc(
                    shared_done["copy_pt", "dve"], 1)

            def copy_xt(p):
                dve.wait_ge(xt_ps, p + 1)
                nc.vector.tensor_copy(xT[:, p, :, :], xt_bank[:, 0:CH * 128]).then_inc(
                    shared_done["copy_xt", "dve"], 1)

            def split_high(p):
                dve.wait_ge(xn_done, p + 1)
                nc.vector.tensor_copy(parts[:, p, :, :], xn[:, p:p + 1, :].to_broadcast([128, 2, N])).then_inc(
                    shared_done["split_high", "dve"], 1)

            def split_low(task, p, half):
                low_part(dve, nc.vector, p, half).then_inc(shared_done[task, "dve"], 1)

            def split_wk(_):
                dve.wait_ge(wk_high_set, 2)
                for half in range(2):
                    rows = slice(C * half, C * half + C)
                    nc.vector.tensor_tensor(wk_low[rows, :], pt_bank[0][0:C, 0:HID], wk_high[rows, :].bitcast(F32),
                                            ALU.subtract).then_inc(wk_low_set, 1)

            def mask_v(g):
                ps = GROUPS[g]
                n = 2 * len(ps)
                dve.wait_ge(v_ps, g + 1)
                out = V[:, 2 * ps[0]:2 * ps[0] + n, :].rearrange("e b (h d) -> e b h d", d=DH)
                got = chain_banks[g][:, 0:n * BLOCK].rearrange("e (b h d) -> e b h d", b=n, d=DH)
                mask = block_mask[:, :].unsqueeze(1).unsqueeze(3).to_broadcast([128, n, BLOCK // DH, DH])
                nc.vector.tensor_tensor(out, got, mask, ALU.mult).then_inc(v_done, 1)

            def inverse_sums(g):
                lo, hi = 2 * GROUPS[g][0], 2 * GROUPS[g][-1] + 2
                dve.wait_ge(exp_done, hi)
                nc.vector.reciprocal(rsum[:, lo:hi], psum_d[:, lo:hi]).then_inc(rsum_done, 1)

            def scale_b(g):
                ps = GROUPS[g]
                n = 2 * len(ps)
                dve.wait_ge(b_ps, g + 1)
                dve.wait_ge(rsum_done, g + 1)
                nc.vector.tensor_tensor(B[:, ps[0]:ps[-1] + 1, :, :].rearrange("d p h o -> d (p h) o"),
                                        chain_banks[g][:, 0:n * C].rearrange("d (b o) -> d b o", b=n),
                                        rsum[:, 2 * ps[0]:2 * ps[0] + n].unsqueeze(2).to_broadcast([128, n, C]),
                                        ALU.mult).then_inc(b_done, 1)

            def copy_m(g):
                half, ps = 0, GROUPS[g]
                rows = slice(C * half, C * half + C)
                dve.wait_ge(m_ps, g + 1)
                dve.wait_ge(mt_zero, 1)
                nc.vector.tensor_copy(MT[rows, ps[0]:ps[-1] + 1, half, :],
                                      chain_banks[g][rows, 0:len(ps) * C]).then_inc(m_done[half], 1)

            def residual(p):
                dve.wait_ge(y_ps, p + 1)
                if p == 0:
                    dve.wait_ge(bias_in, 32)
                nc.vector.scalar_tensor_tensor(y_sb[:, p, :], y_banks[p][:, 0:N], bias[:, :], x_sb[:, p, :],
                                               ALU.add, ALU.add).then_inc(y_done, 1)

            nc.vector.memset(zeros[:, :], 0.0).then_inc(zeros_set, 1)
            nc.vector.memset(wkT[:, :, :], 0.0).then_inc(pad_zero, 1)
            nc.vector.memset(wvT[:, :, :], 0.0).then_inc(pad_zero, 1)
            nc.vector.memset(neg_power[:, :], -0.5).then_inc(small_set, 1)
            nc.vector.memset(eps_row[:, :, 0], 0.0).then_inc(small_set, 1)
            nc.vector.memset(eps_row[:, :, 1], -EPS).then_inc(small_set, 1)
            dve.wait_ge(ident_set, 1)
            columns = ident[:, :].rearrange("p (g j) -> p g j", j=PER_GROUP)
            nc.vector.tensor_tensor(same_group[:, :, :], columns[:, :, 0:1].to_broadcast([128, 64, PER_GROUP]),
                                    columns[:, :, 1:2].to_broadcast([128, 64, PER_GROUP]), ALU.add).then_inc(same_set, 1)
            dve.wait_ge(small_set, 3)
            dve.wait_ge(mask_set, 1)
            nc.vector.tensor_reduce(block_mask[:, :], head_mask[:, :].rearrange("e (q h) -> e h q", h=BLOCK // DH), X,
                                    ALU.add).then_inc(block_set, 1)
            dve.wait_ge(block_set, 1)

            run = {"moments": moments, "aggregate": aggregate, "scale_means": scale_means,
                   "deviation": deviation, "variance": variance, "normalise": normalise, "maxima": maxima,
                   "inverse_sums": inverse_sums, "scale_b": scale_b, "copy_m": copy_m, "residual": residual,
                   "copy_pt": copy_pt, "copy_xt": copy_xt, "split_high": split_high, "split_wk": split_wk,
                   "split_low_a": lambda p: split_low("split_low_a", p, 0),
                   "split_low_b": lambda p: split_low("split_low_b", p, 1), "mask_v": mask_v}
            for task, i in tasks(DVE_ORDER):
                run[task](i)

        @block.tensor
        def _(pe):
            def warm(n):
                for _ in range(n):
                    nc.tensor.matmul(y_bank[:, 0:256], zeros[:, 0:128], zeros[:, :], start=True, stop=True)

            def wait_left(bank):
                if bank is xt_bank:
                    wait_shared(pe, "copy_xt", PAIRS - 1)
                for i in range(2):
                    if bank is k_bank[i]:
                        pe.wait_ge(exp_done, 2 * (PAIRS - 1 + i))
                    if bank is pt_bank[i]:
                        wait_shared(pe, "copy_pt", PAIRS - 2 + i)

            def transpose_x(p):
                pe.wait_ge(xn_done, p + 1)
                if p >= 1:
                    wait_shared(pe, "copy_xt", p - 1)
                for ch in range(CH):
                    last = nc.tensor.transpose(xt_bank[:, ch * 128:(ch + 1) * 128],
                                               xn[:, p, ch * 128:(ch + 1) * 128], ident[:, :])
                last.then_inc(xt_ps, 1)

            def keys(p):
                if p >= 2:
                    pe.wait_ge(exp_done, 2 * (p - 1))
                if p < WHOLE:
                    pe.wait_ge(xn_done, p + 1)
                    if p == 0:
                        pe.wait_ge(wkT_set, 2)
                    for half in range(2):
                        last = nc.tensor.matmul(k_bank[p % 2][:, half * N:(half + 1) * N], wkT[:, half, :],
                                                xn[:, p, :], start=True, stop=True)
                else:
                    wait_shared(pe, "split_low_a", p)
                    wait_shared(pe, "split_low_b", p)
                    if p == WHOLE:
                        pe.wait_ge(wk_low_set, 2)
                    nc.tensor.matmul(k_bank[p % 2][:, :], wk_high[:, :], parts[:, p, :, :], start=True, stop=False)
                    last = nc.tensor.matmul(k_bank[p % 2][:, :], wk_low[:, :], parts[:, p, :, :],
                                            start=False, stop=True)
                last.then_inc(k_ps, 1)

            def transpose_p(p):
                pe.wait_ge(exp_done, 2 * p + 2)
                if p == 0:
                    pe.wait_ge(wk_low_set, 2)
                if p == 1:
                    pe.wait_ge(woT_set, 1)
                if p >= 2:
                    wait_shared(pe, "copy_pt", p - 2)
                for half in range(2):
                    for ch in range(CH):
                        c0 = (half * CH + ch) * 128
                        last = nc.tensor.transpose(pt_bank[p % 2][:, c0:c0 + 128],
                                                   P[:, 2 * p + half, ch * 128:(ch + 1) * 128], ident[:, :])
                last.then_inc(pt_ps, 1)

            def context(p):
                g = group_of[p]
                wait_shared(pe, "copy_pt", p)
                wait_shared(pe, "copy_xt", p)
                if p == 0:
                    pe.wait_ge(gmv_done, len(STATS))
                elif p == GROUPS[g][0]:
                    pe.wait_ge(at_done, g)
                c0 = (p - GROUPS[g][0]) * HID
                for ch in range(CH):
                    for half in range(2):
                        rows = slice(C * half, C * half + C)
                        last = nc.tensor.matmul(at_bank[rows, c0:c0 + HID], xT[:, p, ch, rows], PT[:, p, half, ch, :],
                                                start=(ch == 0), stop=(ch == CH - 1))
                last.then_inc(at_ps, 1)

            def values(g):
                ps = GROUPS[g]
                pe.wait_ge(at_done, g + 1)
                if g == 0:
                    pe.wait_ge(wvT_set, 2)
                wait_left(chain_banks[g])
                earlier = [q for q in range(g) if chain_banks[q] is chain_banks[g]]
                if earlier:
                    for half in range(2):
                        pe.wait_ge(m_done[half], earlier[-1] + 1)
                out = chain_banks[g][:, 0:2 * len(ps) * BLOCK].rearrange("e (p h d) -> e p h d", h=2, d=BLOCK)
                for half in range(2):
                    for q in range(BLOCKS):
                        rows = slice(BLOCK * q, BLOCK * q + BLOCK)
                        last = nc.tensor.matmul(out[rows, :, half, :], wvT[:, half, rows],
                                                AT[:, ps[0]:ps[-1] + 1, rows], start=True, stop=True)
                last.then_inc(v_ps, 1)

            def mix(g):
                ps = GROUPS[g]
                pe.wait_ge(v_done, g + 1)
                if g == 0:
                    pe.wait_ge(woT_set, 1)
                for i, b in enumerate(range(2 * ps[0], 2 * ps[-1] + 2)):
                    for q in range(BLOCKS):
                        rows = slice(BLOCK * q, BLOCK * q + BLOCK)
                        last = nc.tensor.matmul(chain_banks[g][rows, i * C:i * C + C], V[rows, b, :], woT[rows, :],
                                                start=True, stop=True)
                last.then_inc(b_ps, 1)

            def project(g):
                ps = GROUPS[g]
                pe.wait_ge(b_done, g + 1)
                if g == 0:
                    pe.wait_ge(w_in, 16)
                for half in range(2):
                    last = nc.tensor.matmul(chain_banks[g][C * half:C * half + C, 0:len(ps) * C], wq,
                                            B[:, ps[0]:ps[-1] + 1, half, :], start=True, stop=True)
                last.then_inc(m_ps, 1)

            def outputs(p):
                g = group_of[p]
                for half in range(2):
                    pe.wait_ge(m_done[half], g + 1)
                earlier = [q for q in range(p) if y_banks[q] is y_banks[p]]
                if earlier:
                    pe.wait_ge(y_done, earlier[-1] + 1)
                wait_left(y_banks[p])
                nc.tensor.matmul(y_banks[p][:, 0:N], MT[:, p, :, :], xn[:, p, :],
                                 start=True, stop=True).then_inc(y_ps, 1)

            def group_means(i):
                ps = STATS[i]
                lo, hi = ps[0], ps[-1] + 1
                pe.wait_ge(mv_done, hi)
                if i == 0:
                    pe.wait_ge(same_set, 1)
                else:
                    pe.wait_ge(gmv_done, i)
                nc.tensor.matmul(at_bank[:, 2 * lo:2 * hi], same_group[:, :, :], mv[:, lo:hi, :],
                                 start=True, stop=True).then_inc(gmean_ps, 1)

            def turn_wk(_):
                pe.wait_ge(ident_set, 1)
                pe.wait_ge(w_in, 16)
                nc.tensor.transpose(pt_bank[0][0:C, 0:HID], wk, ident[:, :]).then_inc(wkT_ps, 1)

            def turn_wo(_):
                pe.wait_ge(wo_in, 16)
                nc.tensor.transpose(pt_bank[1][:, 0:C], wo[:, :], ident[0:C, 0:C]).then_inc(woT_ps, 1)

            def turn_wv(_):
                pe.wait_ge(ident_set, 1)
                pe.wait_ge(w_in, 16)
                nc.tensor.transpose(chain_bank[0:C, 0:HID], wv, ident[:, :]).then_inc(wvT_ps, 1)

            pe.wait_ge(zeros_set, 1)
            run = {"turn_wk": turn_wk, "turn_wo": turn_wo, "group_means": group_means, "turn_wv": turn_wv,
                   "keys": keys, "transpose_x": transpose_x, "transpose_p": transpose_p, "context": context,
                   "values": values, "mix": mix, "project": project, "outputs": outputs}
            for task, i in tasks(PE_ORDER):
                warm(WARM.get((task, i), 0))
                run[task](i)


def kernel(x, L0_conv_w_qkv, L0_conv_w_out, L0_conv_b_out):
    import numpy as np
    import concourse.bacc as bacc
    from concourse.bass_utils import run_bass_kernel_spmd

    nc = bacc.Bacc("TRN2", target_bir_lowering=False, num_devices=1)
    batch, c, h, w = x.shape
    arrays = {
        "x": np.ascontiguousarray(x).reshape(batch, c, h * w),
        "w_qkv": np.ascontiguousarray(L0_conv_w_qkv),
        "w_out": np.ascontiguousarray(L0_conv_w_out),
        "b_out": np.ascontiguousarray(L0_conv_b_out).reshape(c, 1),
    }
    args = [nc.dram_tensor(n, a.shape, mybir.dt.from_np(a.dtype), kind="ExternalInput").ap() for n, a in arrays.items()]
    y = nc.dram_tensor("y", (batch, c, h * w), mybir.dt.float32, kind="ExternalOutput").ap()
    attention_kernel(nc, *args, y)
    r = run_bass_kernel_spmd(nc, [arrays], core_ids=[0])
    return r.results[0]["y"].reshape(batch, c, h, w)
```
